# Optimizing a Trainium2 kernel written in Bass

```python
import numpy as np
import jax
import jax.numpy as jnp

def _softmax(x, axis=-1):
    return jax.nn.softmax(x, axis=axis)
def _gelu(x):
    return jax.nn.gelu(x, approximate=True)
def _silu(x):
    return jax.nn.silu(x)
def _sigmoid(x):
    return jax.nn.sigmoid(x)
def _layernorm(x, axis=-1, eps=1e-5):
    m = jnp.mean(x, axis=axis, keepdims=True)
    v = jnp.var(x, axis=axis, keepdims=True)
    return (x - m) / jnp.sqrt(v + eps)
def _scatter_add(tgt, idx, src, axis=0):
    return tgt.at[idx].add(src)
def _segment_sum(src, seg, n):
    return jax.ops.segment_sum(src, seg, n)

kernel_name = 'mk_adj_preln_d1_adj_128_438da9'

def setup_inputs(seed: int = 0):
    np.random.seed(seed)
    _w = jnp.asarray
    def _rec_inputs():
        import jax
        import jax.numpy as jnp
        _gk = jax.random.key(seed)
        x = 0.0002279 + 0.9999 * jax.random.normal(jax.random.fold_in(_gk, 1), (8192, 128), jnp.float32)
        _a = jax.random.bernoulli(jax.random.fold_in(_gk, 2), 0.000488281, (8192, 8192))
        adj = _a.astype(jnp.int32)
        return x, adj
    x, adj = _rec_inputs()
    def _L0_gnn_setup():
        import jax, jax.numpy as jnp
        import numpy as np
        N, D = (8192, 128)
        key = jax.random.key(seed)
        k1, k2, k3 = jax.random.split(key, 3)
        adj = jax.random.randint(k1, (N, N), 0, 2, dtype=jnp.int32)
        emb = jax.random.normal(k2, (N, D), dtype=jnp.float32)
        attn = jax.random.normal(k3, (2 * D, 1), dtype=jnp.float32)
        return {'adj': adj, 'emb': emb, 'attn': attn}
    _L0_gnn_all = _L0_gnn_setup()
    _L0_gnn_in = {k: v for k, v in _L0_gnn_all.items() if k in ('attn', )}
    del _L0_gnn_all

    return {
        "x": x,
        "adj": adj,
        "L0_gnn_attn": _L0_gnn_in["attn"],
    }

def reference(x, adj, L0_gnn_attn):
    import jax
    import jax.numpy as jnp
    def _L0_gnn_ref(adj, emb, attn):
        import jax, jax.numpy as jnp
        import numpy as np
        N, D = (8192, 128)
        d = emb.shape[1]
        s_i = emb @ attn[:d]
        s_j = emb @ attn[d:]
        e = jax.nn.leaky_relu(s_i + s_j.T, negative_slope=0.2)
        neg_inf = jnp.float32(-1000000000.0)
        e = e + jnp.where(adj > 0, jnp.float32(0.0), neg_inf)
        alpha = jax.nn.softmax(e, axis=1)
        return alpha @ emb

    h = jnp.maximum(_layernorm(x, axis=-1), 0.0)
    x = x + _L0_gnn_ref(adj, h, L0_gnn_attn)
    return x


_drawn_inputs = setup_inputs


def setup_inputs(seed=0):
    import zlib

    import numpy as np

    out = dict(_drawn_inputs(seed))
    spreads = {}
    factors = {}
    for name, (base, spread) in spreads.items():
        noise = np.random.default_rng([zlib.crc32(name.encode()), seed]).standard_normal(out[name].shape)
        drawn = base * np.exp(spread * noise) if base else spread * noise
        out[name] = jnp.asarray(drawn.astype(out[name].dtype))
    for name, factor in factors.items():
        out[name] = (out[name] * factor).astype(out[name].dtype)
    return out
```

```python
import concourse.bass as bass
from concourse import mybir
from contextlib import ExitStack


def graph_attention_kernel(nc: bass.Bass, x: bass.AP, adj: bass.AP, attn: bass.AP, out: bass.AP):
    fp32, bf16, i32 = mybir.dt.float32, mybir.dt.bfloat16, mybir.dt.int32
    ALU = mybir.AluOpType
    ACT = mybir.ActivationFunctionType
    AX = mybir.AxisListType
    ds = bass.ds

    P = 128
    N, D = x.shape
    TILES = N // P
    PAIRS = TILES // 2
    HALF = N // 2
    CHUNKS = 8
    WORDS = N // CHUNKS
    BANK = 512
    BANKS = WORDS // BANK
    QUARTERS = 4
    PART = WORDS // QUARTERS
    CAND = 8 * QUARTERS
    SLOTS = 8
    BIAS = (2 ** CHUNKS - 1) * WORDS // 2
    COLS = D + 4
    SJ, SI, ONE = D, D + 1, D + 2
    FAR = 2 * N
    MASKED = -1.0e9
    NOTHING = -1.0e30
    EPS = 1e-5
    XC = 4
    XT = TILES // XC
    LC = 4
    LW = N // LC
    GB = BANK // P
    GROUPS = N // BANK

    table = nc.dram_tensor("h_table", [N, COLS], fp32).ap()
    sj_row = nc.dram_tensor("sj_row", [TILES, P], fp32).ap()
    row_list = nc.dram_tensor("row_list", [N + P, 1], i32).ap()

    x_t = x.rearrange("(t p) d -> p t d", p=P)
    out_t = out.rearrange("(t p) d -> p t d", p=P)
    adj_t = adj.rearrange("(t p) c -> t p c", p=P)
    table_t = table.rearrange("(t p) c -> p t c", p=P)

    ctx = ExitStack()
    with ctx:
        def sb(name, shape, dt):
            return ctx.enter_context(nc.sbuf_tensor(name, shape, dt))

        def pb(name, shape, dt):
            return ctx.enter_context(nc.psum_tensor(name, shape, dt))

        def sem(name):
            return ctx.enter_context(nc.semaphore(name))

        adj_ring = sb("adj_ring", [P, 4, HALF], i32)
        sign_ring = sb("sign_ring", [P, 4, HALF], bf16)
        h_all = sb("h_all", [P, TILES, COLS], fp32)
        x_all = sb("x_all", [P, TILES, D], fp32)
        near = sb("near", [P, 2, 2 * SLOTS, COLS], fp32)
        mixed_rows = sb("mixed_rows", [P, 2, 2, D], fp32)

        attn_b = sb("attn_b", [P, 2 * D], fp32)
        stats = sb("stats", [P, TILES, 6], fp32)
        mean = sb("mean", [P, TILES], fp32)
        var = sb("var", [P, TILES], fp32)
        gap = sb("gap", [P, TILES], fp32)
        rstd = sb("rstd", [P, TILES], fp32)
        shift = sb("shift", [P, TILES], fp32)
        sj_t = sb("sj_t", [TILES, P], fp32)

        pack_w = sb("pack_w", [P, CHUNKS, P], bf16)
        place_w = sb("place_w", [64, P], bf16)
        place = sb("place", [64, WORDS], bf16)
        before = sb("before", [P, P], bf16)
        ones = sb("ones", [P, P], bf16)
        ident = sb("ident", [P, P], fp32)
        bit_mask = sb("bit_mask", [P, CHUNKS], i32)
        bit_col = sb("bit_col", [P, CHUNKS], i32)
        row_id = sb("row_id", [P, TILES], i32)
        far_row = sb("far_row", [P, TILES + 1], i32)

        cand = sb("cand", [P, 2 * CAND], fp32)
        cand_i = sb("cand_i", [P, 2 * CAND], i32)
        word_at = sb("word_at", [P, 2 * CAND], i32)
        bits = sb("bits", [P, 2, 2 * CAND * CHUNKS], i32)
        cols1 = sb("cols1", [P, 2 * CAND * CHUNKS], fp32)
        hits = sb("hits", [P, 2 * CAND * CHUNKS], fp32)
        best = sb("best", [P, 2 * SLOTS], fp32)
        empty_far = sb("empty_far", [P, 2 * SLOTS], fp32)
        empty_pen = sb("empty_pen", [P, 2, 2 * SLOTS], fp32)
        near_id = sb("near_id", [P, 2, 2 * SLOTS], i32)
        fullest = sb("fullest", [P, 2, 2], fp32)
        count_junk = sb("count_junk", [P, 2, 2 * CAND * CHUNKS], bf16)
        degree = sb("degree", [P, 2, 2], fp32)

        score = sb("score", [P, 2 * SLOTS], fp32)
        leaky = sb("leaky", [P, 2 * SLOTS], fp32)
        top = sb("top", [P, 2], fp32)
        below = sb("below", [P, 2 * SLOTS], fp32)
        weight = sb("weight", [P, 2 * SLOTS], fp32)
        weight_n = sb("weight_n", [P, 2 * SLOTS], fp32)
        total = sb("total", [P, 2], fp32)
        inv = sb("inv", [P, 2], fp32)
        outside = sb("outside", [P, 2], fp32)
        crowded = sb("crowded", [P, 2], fp32)
        flag = sb("flag", [P, 2, 2], bf16)
        flags_before = sb("flags_before", [P, 2, 2], bf16)
        flags_all = sb("flags_all", [P, 1], bf16)
        unlisted = sb("unlisted", [P, 2], fp32)
        list_at = sb("list_at", [P, 2, 2], i32)
        list_row = sb("list_row", [P, 2, 2], i32)
        listed_i = sb("listed_i", [P, 1], i32)
        listed_r = sb("listed_r", [P, 1], i32)
        batches = sb("batches", [P, 1], i32)

        far_id = sb("far_id", [P, 1], i32)
        far_tab = sb("far_tab", [P, COLS], fp32)
        far_x = sb("far_x", [P, D], fp32)
        part_top = sb("part_top", [P, LC], fp32)
        neg_top = sb("neg_top", [P, 1], fp32)
        p_t = sb("p_t", [P, 2, BANK], fp32)
        far_inv = sb("far_inv", [P, 1], fp32)
        far_out = sb("far_out", [P, D], fp32)

        mask_rows = adj_ring[:, 0:2, :].rearrange("p a b -> p (a b)")
        mask_f = mask_rows.bitcast(fp32)
        sj_all = adj_ring[:, 2:4, :].rearrange("p a b -> p (a b)").bitcast(fp32)
        logits = sign_ring[:, :, :].rearrange("p a b -> p (a b)").bitcast(fp32)
        products = logits

        words = [pb(f"words{i}", [P, WORDS], fp32) for i in range(2)]
        rank = pb("rank", [P, BANK], fp32)
        far_t = [pb(f"far_t{i}", [P, BANK], fp32) for i in range(2)]
        far_sum = pb("far_sum", [P, BANK], fp32)

        half_neg = sb("half_neg", [P, 1], fp32)

        x_in = [sem(f"x_in{i}") for i in range(XC)]
        attn_in = sem("attn_in")
        adj_in = [sem(f"adj_in{i}") for i in range(4)]
        dve_passed = sem("dve_passed")
        pool_passed = sem("pool_passed")
        setup = sem("setup")
        stat_done = sem("stat_done")
        dots = sem("dots")
        flag_done = sem("flag_done")
        place_done = sem("place_done")
        std_ready = sem("std_ready")
        h_ready = sem("h_ready")
        table_ready = sem("table_ready")
        sj_turned = sem("sj_turned")
        sj_t_ready = sem("sj_t_ready")
        table_out = sem("table_out")
        sj_out = sem("sj_out")
        consts = sem("consts")
        zeroed = sem("zeroed")
        list_out = sem("list_out")
        signed = sem("signed")
        packed = sem("packed")
        maxed = sem("maxed")
        find = sem("find")
        bits_ready = sem("bits_ready")
        counted = sem("counted")
        near_id_ready = sem("near_id_ready")
        near_in = [sem(f"near_in{i}") for i in range(2)]
        mix = sem("mix")
        below_ready = sem("below_ready")
        weight_ready = sem("weight_ready")
        flags_ready = sem("flags_ready")
        ranked = sem("ranked")
        list_at_ready = sem("list_at_ready")
        list_in = [sem(f"list_in{i}") for i in range(2)]
        pair_mixed = sem("pair_mixed")
        stored = [sem(f"stored{i}") for i in range(2)]
        total_ready = sem("total_ready")
        batches_ready = sem("batches_ready")
        sj_all_in = sem("sj_all_in")
        far_id_in = sem("far_id_in")
        far_tab_in = sem("far_tab_in")
        far_x_in = sem("far_x_in")
        far_adj_in = sem("far_adj_in")
        raw_ready = sem("raw_ready")
        long_step = sem("long_step")
        neg_top_ready = sem("neg_top_ready")
        exp_ready = sem("exp_ready")
        turned = sem("turned")
        p_t_ready = [sem(f"p_t_ready{i}") for i in range(2)]
        p_t_used = sem("p_t_used")
        far_sum_ready = sem("far_sum_ready")
        far_out_ready = sem("far_out_ready")
        far_stored = sem("far_stored")

        FIND = 8
        MIX = 22

        block = ctx.enter_context(nc.Block())

        @block.sync
        def _(sp):
            for c in range(XC):
                sp.dma_start(x_all[:, c * XT:(c + 1) * XT, :], x_t[:, c * XT:(c + 1) * XT, :]).then_inc(x_in[c], 16)
            sp.dma_start(attn_b[:, :], attn.rearrange("d o -> o d").broadcast_to([P, 2 * D])).then_inc(attn_in, 16)

            def load_half(p, s):
                sp.dma_start(adj_ring[:, s, :], adj_t[2 * p + s // 2, :, (s % 2) * HALF:(s % 2 + 1) * HALF]) \
                    .then_inc(adj_in[s], 16)

            def load_pair(p):
                for s in range(4):
                    sp.wait_ge(signed, 4 * p + s - 3)
                    load_half(p, s)

            def store_pair(q, e):
                sp.wait_ge(pair_mixed, q + 1)
                sp.dma_start(out_t[:, ds(2 * q, 2), :], mixed_rows[:, e, :, :]).then_inc(stored[e], 16)

            for s in range(4):
                load_half(0, s)
            load_pair(1)
            sp.wait_ge(table_ready, 1)
            sp.dma_start(table_t, h_all[:, :, :]).then_inc(table_out, 16)
            sp.wait_ge(sj_t_ready, 1)
            sp.dma_start(sj_row, sj_t[:, :]).then_inc(sj_out, 16)
            load_pair(2)
            load_pair(3)
            store_pair(0, 0)
            with sp.Fori(2, PAIRS // 2) as i:
                for e in range(2):
                    load_pair(2 * i + e)
                    store_pair(2 * i + e - 3, (e + 1) % 2)
            for q in range(PAIRS - 3, PAIRS):
                store_pair(q, q % 2)
                if q == PAIRS - 3:
                    sp.wait_ge(signed, 4 * PAIRS)
                    sp.wait_ge(sj_out, 16)
                    sp.dma_start(sj_all, sj_row.rearrange("t p -> (t p)").rearrange("(o n) -> o n", o=1)
                                 .broadcast_to([P, N])).then_inc(sj_all_in, 16)

        @block.gpsimd
        def _(pool):
            nc.gpsimd.memset(ident[:, :], 0.0)
            nc.gpsimd.memset(ones[:, :], 1.0)
            nc.gpsimd.memset(pack_w[:, :, :], 0.0)
            nc.gpsimd.memset(place_w[:, :], 1.0)
            nc.gpsimd.memset(place[:, :], 0.0)
            nc.gpsimd.memset(far_row[:, :], FAR).then_inc(zeroed, 1)
            pool.wait_ge(zeroed, 1)
            nc.gpsimd.affine_select(out=ident[:, :], in_=ident[:, :], compare_op=ALU.not_equal, fill=1.0,
                                    base=0, pattern=[[-1, P]], channel_multiplier=1)
            nc.gpsimd.affine_select(out=before[:, :], in_=ones[:, :], compare_op=ALU.is_gt, fill=0.0,
                                    base=0, pattern=[[1, P]], channel_multiplier=-1)
            for c in range(CHUNKS):
                last = nc.gpsimd.affine_select(out=pack_w[:, c, :], in_=pack_w[:, c, :], compare_op=ALU.not_equal,
                                               fill=float(2 ** c * WORDS // 2), base=0, pattern=[[-1, P]],
                                               channel_multiplier=1)
            last.then_inc(zeroed, 1)
            pool.wait_ge(zeroed, 2)
            nc.gpsimd.iota(place[0:32, :], pattern=[[1, WORDS // 32], [0, 32]], base=0, channel_multiplier=0,
                           allow_small_or_imprecise_dtypes=True).then_inc(zeroed, 1)
            pool.wait_ge(zeroed, 3)
            nc.gpsimd.iota(place[32:33, :], pattern=[[0, WORDS // 32], [1, 32]], base=0, channel_multiplier=0,
                           allow_small_or_imprecise_dtypes=True).then_inc(zeroed, 1)
            pool.wait_ge(zeroed, 4)
            for c in range(CHUNKS):
                nc.gpsimd.memset(bit_mask[:, c:c + 1], 2 ** c * WORDS)
            nc.gpsimd.iota(bit_col[:, :], pattern=[[WORDS, CHUNKS]], base=1, channel_multiplier=0)
            nc.gpsimd.memset(near[:, :, :, :], 0.0)
            nc.gpsimd.memset(far_tab[:, :], 0.0)
            nc.gpsimd.memset(far_x[:, :], 0.0)
            nc.gpsimd.memset(half_neg[:, :], -0.5)
            nc.gpsimd.iota(row_id[:, :], pattern=[[P, TILES]], base=0, channel_multiplier=1).then_inc(consts, 1)
            pool.wait_ge(consts, 1)
            pool.dma_start(row_list.rearrange("(p t) o -> p (t o)", p=P), far_row[:, :]).then_inc(list_out, 16)
            pool.wait_ge(list_out, 16)
            pool.wait_ge(table_out, 16)

            last_row = pool.to_reg(N - 1)

            def gather_pair(p, e):
                pool.wait_ge(near_id_ready, p + 1)
                pool.sem_inc(pool_passed, 1)
                for k in range(2 * SLOTS):
                    pool.indirect_dma_start(
                        out=near[:, e, k, :], out_offset=None, in_=table,
                        in_offset=bass.IndirectOffsetOnAxis(ap=near_id[:, e, k:k + 1], axis=0),
                        bounds_check=last_row, oob_is_err=False).then_inc(near_in[e], 16)

            def list_pair(q, e):
                pool.wait_ge(list_at_ready, q + 1)
                pool.sem_inc(pool_passed, 1)
                for a in range(2):
                    pool.indirect_dma_start(
                        out=row_list, out_offset=bass.IndirectOffsetOnAxis(ap=list_at[:, e, a:a + 1], axis=0),
                        in_=list_row[:, e, a:a + 1], in_offset=None,
                        bounds_check=last_row, oob_is_err=False).then_inc(list_in[e], 16)

            gather_pair(0, 0)
            gather_pair(1, 1)
            with pool.Fori(1, PAIRS // 2) as i:
                for e in range(2):
                    pool.wait_ge(pair_mixed, 2 * i + e - 1)
                    gather_pair(2 * i + e, e)
                    list_pair(2 * i + e - 2, e)
            list_pair(PAIRS - 2, 0)
            list_pair(PAIRS - 1, 1)

            for e in range(2):
                pool.wait_ge(list_in[e], 16 * PAIRS)
                pool.wait_ge(stored[e], 8 * PAIRS)
            pool.wait_ge(signed, 4 * PAIRS)
            pool.wait_ge(batches_ready, 1)
            n_batches = pool.value_load(batches[0:1, 0:1], min_val=1, max_val=TILES)
            with pool.Fori(0, n_batches) as b:
                pool.dma_start(far_id[:, :], row_list[ds(b * P, P), :]).then_inc(far_id_in, 16)
                pool.wait_ge(far_id_in, 16 * b + 16)
                pool.sem_inc(pool_passed, 1)
                for dst, src, done in ((mask_rows, adj, far_adj_in), (far_tab[:, :], table, far_tab_in),
                                       (far_x[:, :], x, far_x_in)):
                    pool.indirect_dma_start(
                        out=dst, out_offset=None, in_=src,
                        in_offset=bass.IndirectOffsetOnAxis(ap=far_id[:, 0:1], axis=0),
                        bounds_check=last_row, oob_is_err=False).then_inc(done, 16)
                pool.wait_ge(far_out_ready, b + 1)
                pool.sem_inc(pool_passed, 1)
                pool.indirect_dma_start(
                    out=out, out_offset=bass.IndirectOffsetOnAxis(ap=far_id[:, 0:1], axis=0),
                    in_=far_out[:, :], in_offset=None,
                    bounds_check=last_row, oob_is_err=False).then_inc(far_stored, 16)
                pool.wait_ge(far_stored, 16 * b + 16)

        @block.scalar
        def _(act):
            act.wait_ge(consts, 1)

            def sign_tile(p, a, first=False):
                for s in (2 * a, 2 * a + 1):
                    act.wait_ge(adj_in[s], 16 * p + 16)
                    if not first:
                        act.wait_ge(packed, 4 * p + s - 3)
                    nc.scalar.activation(sign_ring[:, s, :], adj_ring[:, s, :], ACT.Sign, bias=half_neg[:, :]) \
                        .then_inc(signed, 1)

            def count_pair(p, e):
                act.wait_ge(bits_ready, p + 1)
                w = CAND * CHUNKS
                for a in range(2):
                    nc.scalar.activation(count_junk[:, e, a * w:(a + 1) * w], bits[:, e, a * w:(a + 1) * w], ACT.Sign,
                                         accum_out=degree[:, e, a:a + 1]).then_inc(counted, 1)

            def exp_pair(p):
                act.wait_ge(below_ready, p + 1)
                nc.scalar.activation(weight[:, :], below[:, :], ACT.Exp).then_inc(weight_ready, 1)

            act.wait_ge(setup, 8)
            nc.scalar.activation(rstd[:, :], var[:, :], ACT.Sqrt).then_inc(std_ready, 1)
            act.wait_ge(setup, 10)
            with act.Fori(0, TILES // 4) as i:
                for u in range(4):
                    t = 4 * i + u
                    nc.scalar.activation(h_all[:, t, 0:D], x_all[:, t, :], ACT.Relu,
                                         bias=shift[:, ds(t, 1)], scale=rstd[:, ds(t, 1)]) \
                        .then_inc(h_ready, 1)
            act.wait_ge(table_ready, 1)
            sign_tile(0, 0, True)
            sign_tile(0, 1, True)
            sign_tile(1, 0)
            sign_tile(1, 1)
            count_pair(0, 0)
            with act.Fori(1, PAIRS // 2) as i:
                for e in range(2):
                    sign_tile(2 * i + e, 0)
                    exp_pair(2 * i + e - 2)
                    sign_tile(2 * i + e, 1)
                    count_pair(2 * i + e - 1, (e + 1) % 2)
            exp_pair(PAIRS - 2)
            count_pair(PAIRS - 1, 1)
            exp_pair(PAIRS - 1)

            act.wait_ge(sj_all_in, 16)
            act.wait_ge(packed, 4 * PAIRS)
            act.wait_ge(batches_ready, 1)
            n_batches = act.value_load(batches[0:1, 0:1], min_val=1, max_val=TILES)
            with act.Fori(0, n_batches) as b:
                act.wait_ge(far_tab_in, 16 * b + 16)
                for c in range(LC):
                    nc.scalar.activation(logits[:, c * LW:(c + 1) * LW], sj_all[:, c * LW:(c + 1) * LW], ACT.Identity,
                                         bias=far_tab[:, SI:SI + 1]).then_inc(raw_ready, 1)
                act.wait_ge(neg_top_ready, b + 1)
                for c in range(LC):
                    nc.scalar.activation(logits[:, c * LW:(c + 1) * LW], logits[:, c * LW:(c + 1) * LW], ACT.Exp,
                                         bias=neg_top[:, 0:1]).then_inc(exp_ready, 1)
                for g in range(0, GROUPS, 2):
                    act.wait_ge(turned, GROUPS * b + g + 1)
                    if g >= 2:
                        act.wait_ge(p_t_used, (GROUPS - 1) * b + g - 1)
                    nc.scalar.activation(p_t[:, 0, :], far_t[0][:, :], ACT.Copy).then_inc(p_t_ready[0], 1)

        @block.vector
        def _(dve):
            for c in range(XC):
                dve.wait_ge(x_in[c], 16)
                with dve.Fori(c * XT // 4, (c + 1) * XT // 4) as i:
                    for u in range(4):
                        nc.vector.bn_stats(out=stats[:, 4 * i + u, :], in_=x_all[:, 4 * i + u, :]) \
                            .then_inc(stat_done, 1)
            dve.wait_ge(stat_done, TILES)
            nc.vector.tensor_tensor(mean[:, :], stats[:, :, 1], stats[:, :, 4], ALU.add).then_inc(setup, 1)
            nc.vector.tensor_tensor(gap[:, :], stats[:, :, 1], stats[:, :, 4], ALU.subtract).then_inc(setup, 1)
            nc.vector.tensor_tensor(var[:, :], stats[:, :, 2], stats[:, :, 5], ALU.add).then_inc(setup, 1)
            dve.wait_ge(setup, 3)
            nc.vector.tensor_tensor(gap[:, :], gap[:, :], gap[:, :], ALU.mult).then_inc(setup, 1)
            nc.vector.tensor_scalar(mean[:, :], mean[:, :], 0.5, None, ALU.mult).then_inc(setup, 1)
            nc.vector.tensor_scalar(var[:, :], var[:, :], 1.0 / D, EPS, ALU.mult, ALU.add).then_inc(setup, 1)
            dve.wait_ge(setup, 6)
            nc.vector.tensor_scalar(gap[:, :], gap[:, :], 0.25, None, ALU.mult).then_inc(setup, 1)
            dve.wait_ge(setup, 7)
            nc.vector.tensor_tensor(var[:, :], var[:, :], gap[:, :], ALU.add).then_inc(setup, 1)
            dve.wait_ge(std_ready, 1)
            nc.vector.reciprocal(rstd[:, :], rstd[:, :]).then_inc(setup, 1)
            dve.wait_ge(setup, 9)
            nc.vector.scalar_tensor_tensor(shift[:, :], mean[:, :], -1.0, rstd[:, :], ALU.mult, ALU.mult) \
                .then_inc(setup, 1)
            dve.wait_ge(attn_in, 16)
            nc.vector.memset(h_all[:, :, ONE:ONE + 1], 1.0)
            nc.vector.memset(h_all[:, :, ONE + 1:ONE + 2], 0.0).then_inc(dots, 1)
            n = 1
            for c in range(XC):
                dve.wait_ge(h_ready, (c + 1) * XT)
                rows = h_all[:, c * XT:(c + 1) * XT, 0:D]
                prod = products[:, c * XT * D:(c + 1) * XT * D].rearrange("p (t d) -> p t d", d=D)
                for col, part in ((SI, 0), (SJ, 1)):
                    a_b = attn_b[:, part * D:(part + 1) * D].unsqueeze(1).broadcast_to([P, XT, D])
                    dve.wait_ge(dots, n)
                    nc.vector.tensor_tensor(prod, rows, a_b, ALU.mult).then_inc(dots, 1)
                    dve.wait_ge(dots, n + 1)
                    nc.vector.tensor_reduce(h_all[:, c * XT:(c + 1) * XT, col], prod, AX.X, ALU.add) \
                        .then_inc(dots, 1)
                    n += 2
            dve.wait_ge(dots, n)
            nc.vector.memset(flags_all[:, :], 0.0).then_inc(table_ready, 1)
            dve.wait_ge(sj_turned, 1)
            nc.vector.tensor_copy(sj_t[:, :], rank[0:TILES, 0:P]).then_inc(sj_t_ready, 1)
            dve.wait_ge(consts, 1)

            def find_pair(p, e):
                f = FIND * p
                for a in range(2):
                    dve.wait_ge(packed, 4 * p + 2 * a + 2)
                    dve.sem_inc(dve_passed, 1)
                    for q in range(QUARTERS):
                        last = nc.vector.max(out=cand[:, a * CAND + 8 * q:a * CAND + 8 * q + 8],
                                             in_=words[a][:, q * PART:(q + 1) * PART])
                    last.then_inc(maxed, 1)
                dve.wait_ge(maxed, 2 * p + 2)
                nc.vector.tensor_scalar(cand_i[:, :], cand[:, :], float(BIAS), None, ALU.add).then_inc(find, 1)
                least = cand[:, :].rearrange("p (a q k) -> p a q k", a=2, k=8)[:, :, :, 7]
                nc.vector.tensor_reduce(fullest[:, e, :], least, AX.X, ALU.max).then_inc(find, 1)
                dve.wait_ge(find, f + 2)
                word = cand_i[:, :].unsqueeze(2).broadcast_to([P, 2 * CAND, CHUNKS])
                nc.vector.tensor_tensor(
                    bits[:, e, :].rearrange("p (w c) -> p w c", c=CHUNKS), word,
                    bit_mask[:, :].unsqueeze(1).broadcast_to([P, 2 * CAND, CHUNKS]), ALU.bitwise_and) \
                    .then_inc(bits_ready, 1)
                nc.vector.tensor_scalar(word_at[:, :], cand_i[:, :], WORDS - 1, None, ALU.bitwise_and) \
                    .then_inc(find, 1)
                dve.wait_ge(find, f + 3)
                nc.vector.tensor_tensor(
                    cols1[:, :].rearrange("p (w c) -> p w c", c=CHUNKS),
                    word_at[:, :].unsqueeze(2).broadcast_to([P, 2 * CAND, CHUNKS]),
                    bit_col[:, :].unsqueeze(1).broadcast_to([P, 2 * CAND, CHUNKS]), ALU.add).then_inc(find, 1)
                dve.wait_ge(find, f + 4)
                dve.wait_ge(bits_ready, p + 1)
                nc.vector.scalar_tensor_tensor(hits[:, :], bits[:, e, :], 0.0, cols1[:, :], ALU.is_gt, ALU.mult) \
                    .then_inc(find, 1)
                dve.wait_ge(find, f + 5)
                dve.sem_inc(dve_passed, 1)
                w = CAND * CHUNKS
                for a in range(2):
                    last = nc.vector.max(out=best[:, a * SLOTS:(a + 1) * SLOTS], in_=hits[:, a * w:(a + 1) * w])
                last.then_inc(find, 1)
                dve.wait_ge(find, f + 6)
                nc.vector.tensor_scalar(empty_pen[:, e, :], best[:, :], 0.0, NOTHING, ALU.is_equal, ALU.mult) \
                    .then_inc(find, 1)
                nc.vector.tensor_scalar(empty_far[:, :], best[:, :], 0.0, float(FAR), ALU.is_equal, ALU.mult) \
                    .then_inc(find, 1)
                dve.wait_ge(find, f + 8)
                nc.vector.scalar_tensor_tensor(near_id[:, e, :], best[:, :], -1.0, empty_far[:, :],
                                               ALU.add, ALU.add).then_inc(near_id_ready, 1)

            def list_places(q, e, reuse=True):
                dve.wait_ge(ranked, q + 1)
                if reuse:
                    dve.wait_ge(list_in[e], 16 * q - 16 * e)
                nc.vector.tensor_scalar(unlisted[:, :], flag[:, e, :], float(-FAR), float(FAR), ALU.mult, ALU.add) \
                    .then_inc(place_done, 1)
                nc.vector.tensor_copy(list_row[:, e, :], row_id[:, ds(2 * q, 2)]).then_inc(place_done, 1)
                dve.wait_ge(place_done, 2 * q + 2)
                nc.vector.tensor_tensor(list_at[:, e, :], unlisted[:, :], rank[:, 2 * e:2 * e + 2], ALU.add) \
                    .then_inc(list_at_ready, 1)

            def mix_pair(q, e, first=False, reuse=True, reuse_places=True):
                m = MIX * q
                dve.wait_ge(near_in[e], 128 * q + (256 if e == 0 else 128))
                s_near = near[:, e, :, SJ].rearrange("p (a k) -> p a k", a=2)
                s_own = h_all[:, ds(2 * q, 2), SI:SI + 1].broadcast_to([P, 2, SLOTS])
                nc.vector.tensor_tensor(score[:, :].rearrange("p (a k) -> p a k", a=2), s_near, s_own, ALU.add) \
                    .then_inc(mix, 1)
                dve.wait_ge(mix, m + 1)
                nc.vector.tensor_tensor(score[:, :], score[:, :], empty_pen[:, e, :], ALU.add).then_inc(mix, 1)
                dve.wait_ge(mix, m + 2)
                nc.vector.scalar_tensor_tensor(leaky[:, :], score[:, :], 0.2, score[:, :], ALU.mult, ALU.max) \
                    .then_inc(mix, 1)
                dve.wait_ge(mix, m + 3)
                leaky_k = leaky[:, :].rearrange("p (a k) -> p a k", a=2)
                nc.vector.tensor_reduce(top[:, :], leaky_k, AX.X, ALU.max).then_inc(mix, 1)
                dve.wait_ge(mix, m + 4)
                nc.vector.tensor_tensor(below[:, :].rearrange("p (a k) -> p a k", a=2), leaky_k,
                                        top[:, :].unsqueeze(2).broadcast_to([P, 2, SLOTS]), ALU.subtract) \
                    .then_inc(below_ready, 1)

                dve.wait_ge(counted, 2 * q + 2)
                nc.vector.scalar_tensor_tensor(outside[:, :], degree[:, e, :], -float(SLOTS + 1), degree[:, e, :],
                                               ALU.add, ALU.mult).then_inc(flag_done, 1)
                nc.vector.tensor_scalar(crowded[:, :], fullest[:, e, :], float(WORDS - BIAS), None, ALU.is_ge) \
                    .then_inc(flag_done, 1)
                dve.wait_ge(flag_done, 5 * q + 2)
                nc.vector.scalar_tensor_tensor(flag[:, e, :], outside[:, :], 0.0, crowded[:, :],
                                               ALU.is_ge, ALU.max).then_inc(flag_done, 1)
                nc.vector.tensor_copy(flags_before[:, e, 0:1], flags_all[:, :]).then_inc(flag_done, 1)
                dve.wait_ge(flag_done, 5 * q + 4)
                nc.vector.tensor_tensor(flags_before[:, e, 1:2], flags_all[:, :], flag[:, e, 0:1], ALU.add) \
                    .then_inc(flag_done, 1)
                dve.wait_ge(flag_done, 5 * q + 5)
                nc.vector.tensor_tensor(flags_all[:, :], flags_before[:, e, 1:2], flag[:, e, 1:2], ALU.add) \
                    .then_inc(flags_ready, 1)
                if not first:
                    list_places(q - 1, 1 - e, reuse_places)

                dve.wait_ge(weight_ready, q + 1)
                weight_k = weight[:, :].rearrange("p (a k) -> p a k", a=2)
                nc.vector.tensor_reduce(total[:, :], weight_k, AX.X, ALU.add).then_inc(mix, 1)
                dve.wait_ge(mix, m + 5)
                nc.vector.reciprocal(inv[:, :], total[:, :]).then_inc(mix, 1)
                dve.wait_ge(mix, m + 6)
                nc.vector.tensor_tensor(weight_n[:, :].rearrange("p (a k) -> p a k", a=2), weight_k,
                                        inv[:, :].unsqueeze(2).broadcast_to([P, 2, SLOTS]), ALU.mult) \
                    .then_inc(mix, 1)
                dve.wait_ge(mix, m + 7)
                if reuse:
                    dve.wait_ge(stored[e], 8 * q - 8 * e)
                done = 7
                for k in range(SLOTS):
                    for a in range(2):
                        acc = mixed_rows[:, e, a, :]
                        base = x_all[:, 2 * q + a, :] if k == 0 else acc
                        if k > 0:
                            dve.wait_ge(mix, m + done - 1)
                        ins = nc.vector.scalar_tensor_tensor(
                            acc, near[:, e, a * SLOTS + k, 0:D], weight_n[:, a * SLOTS + k:a * SLOTS + k + 1], base,
                            ALU.mult, ALU.add)
                        final = k == SLOTS - 1 and a == 1
                        ins.then_inc(pair_mixed if final else mix, 1)
                        done += 1
                assert done - 1 == MIX

            find_pair(0, 0)
            find_pair(1, 1)
            mix_pair(0, 0, first=True, reuse=False)
            find_pair(2, 0)
            mix_pair(1, 1, reuse=False, reuse_places=False)
            find_pair(3, 1)
            mix_pair(2, 0, reuse_places=False)
            with dve.Fori(2, PAIRS // 2) as i:
                find_pair(2 * i, 0)
                mix_pair(2 * i - 1, 1)
                find_pair(2 * i + 1, 1)
                mix_pair(2 * i, 0)
            mix_pair(PAIRS - 1, 1)
            list_places(PAIRS - 1, 1)

            dve.wait_ge(total_ready, 1)
            nc.vector.tensor_scalar(listed_i[:, :], rank[:, 8:9], float(P - 1), float(P), ALU.add, ALU.max) \
                .then_inc(long_step, 1)
            dve.wait_ge(long_step, 1)
            nc.vector.tensor_scalar(batches[:, :], listed_i[:, :], P.bit_length() - 1, None,
                                    ALU.arith_shift_right).then_inc(batches_ready, 1)

            dve.wait_ge(batches_ready, 1)
            n_batches = dve.value_load(batches[0:1, 0:1], min_val=1, max_val=TILES)
            LONG = 3 * LC + 1
            with dve.Fori(0, n_batches) as b:
                s = LONG * b + 1
                dve.wait_ge(far_adj_in, 16 * b + 16)
                for c in range(LC):
                    nc.vector.tensor_scalar(mask_f[:, c * LW:(c + 1) * LW], mask_rows[:, c * LW:(c + 1) * LW], 0.0,
                                            MASKED, ALU.is_le, ALU.mult).then_inc(long_step, 1)
                for c in range(LC):
                    dve.wait_ge(raw_ready, LC * b + c + 1)
                    nc.vector.scalar_tensor_tensor(logits[:, c * LW:(c + 1) * LW], logits[:, c * LW:(c + 1) * LW], 0.2,
                                                   logits[:, c * LW:(c + 1) * LW], ALU.mult, ALU.max) \
                        .then_inc(long_step, 1)
                for c in range(LC):
                    dve.wait_ge(long_step, s + LC + c + 1)
                    dve.sem_inc(dve_passed, 1)
                    nc.vector.tensor_tensor_reduce(
                        out=logits[:, c * LW:(c + 1) * LW], in0=logits[:, c * LW:(c + 1) * LW],
                        in1=mask_f[:, c * LW:(c + 1) * LW], scale=1.0, scalar=-3.0e38, op0=ALU.add, op1=ALU.max,
                        accum_out=part_top[:, c:c + 1]).then_inc(long_step, 1)
                dve.wait_ge(long_step, s + 3 * LC)
                nc.vector.tensor_reduce(neg_top[:, :], part_top[:, :], AX.X, ALU.max, negate=True) \
                    .then_inc(neg_top_ready, 1)
                for g in range(1, GROUPS, 2):
                    dve.wait_ge(turned, GROUPS * b + g + 1)
                    if g >= 2:
                        dve.wait_ge(p_t_used, (GROUPS - 1) * b + g - 1)
                    nc.vector.tensor_copy(p_t[:, 1, :], far_t[1][:, :]).then_inc(p_t_ready[1], 1)
                dve.wait_ge(far_sum_ready, b + 1)
                nc.vector.reciprocal(far_inv[:, :], far_sum[:, ONE:ONE + 1]).then_inc(long_step, 1)
                dve.wait_ge(long_step, s + 3 * LC + 1)
                dve.wait_ge(far_x_in, 16 * b + 16)
                nc.vector.scalar_tensor_tensor(far_out[:, :], far_sum[:, 0:D], far_inv[:, 0:1], far_x[:, :],
                                               ALU.mult, ALU.add).then_inc(far_out_ready, 1)

        @block.tensor
        def _(pe):
            pe.wait_ge(consts, 1)
            pe.wait_ge(table_ready, 1)
            nc.tensor.transpose(rank[0:TILES, 0:P], h_all[:, :, SJ], ident[:, :]).then_inc(sj_turned, 1)

            def pack_tile(p, a, first=False):
                if not first:
                    pe.wait_ge(maxed, 2 * p + a - 1)
                for k in range(BANKS):
                    nc.tensor.matmul(words[a][:, k * BANK:(k + 1) * BANK], place_w[:, :],
                                     place[:, k * BANK:(k + 1) * BANK], start=True, stop=False)
                for c in range(CHUNKS):
                    s, o = 2 * a + c // (CHUNKS // 2), (c % (CHUNKS // 2)) * WORDS
                    if c % (CHUNKS // 2) == 0:
                        pe.wait_ge(signed, 4 * p + s + 1)
                    for k in range(BANKS):
                        last = nc.tensor.matmul(words[a][:, k * BANK:(k + 1) * BANK], pack_w[:, c, :],
                                                sign_ring[:, s, o + k * BANK:o + (k + 1) * BANK],
                                                start=False, stop=(c == CHUNKS - 1))
                    if c % (CHUNKS // 2) == CHUNKS // 2 - 1:
                        last.then_inc(packed, 1)

            def rank_pair(q, e, first=False):
                pe.wait_ge(flags_ready, q + 1)
                if first:
                    pe.wait_ge(sj_t_ready, 1)
                else:
                    pe.wait_ge(list_at_ready, q)
                at = rank[:, 2 * e:2 * e + 2]
                nc.tensor.matmul(at, before[:, :], flag[:, e, :], start=True, stop=False)
                nc.tensor.matmul(at, ones[:, :], flags_before[:, e, :], start=False, stop=True).then_inc(ranked, 1)

            pack_tile(0, 0, True)
            pack_tile(0, 1, True)
            pack_tile(1, 0)
            pack_tile(1, 1)
            pack_tile(2, 0)
            pack_tile(2, 1)
            rank_pair(0, 0, True)
            with pe.Fori(1, PAIRS // 2 - 1) as i:
                for e in (1, 0):
                    pack_tile(2 * i + 2 - e, 0)
                    pack_tile(2 * i + 2 - e, 1)
                    rank_pair(2 * i - e, e)
            pack_tile(PAIRS - 1, 0)
            pack_tile(PAIRS - 1, 1)
            rank_pair(PAIRS - 3, 1)
            rank_pair(PAIRS - 2, 0)
            rank_pair(PAIRS - 1, 1)
            pe.wait_ge(flags_ready, PAIRS)
            pe.wait_ge(list_at_ready, PAIRS)
            nc.tensor.matmul(rank[:, 8:9], ones[:, :], flags_all[:, :], start=True, stop=True) \
                .then_inc(total_ready, 1)

            pe.wait_ge(batches_ready, 1)
            n_batches = pe.value_load(batches[0:1, 0:1], min_val=1, max_val=TILES)
            with pe.Fori(0, n_batches) as b:
                def mix_group(g):
                    pe.wait_ge(p_t_ready[g % 2], GROUPS // 2 * b + g // 2 + 1)
                    for k in range(GB):
                        t = g * GB + k
                        last = nc.tensor.matmul(far_sum[:, 0:ONE + 1], p_t[:, g % 2, k * P:(k + 1) * P],
                                                h_all[:, t, 0:ONE + 1], start=(t == 0), stop=(t == TILES - 1))
                    last.then_inc(far_sum_ready if g == GROUPS - 1 else p_t_used, 1)

                for g in range(GROUPS):
                    pe.wait_ge(exp_ready, LC * b + g * LC // GROUPS + 1)
                    for k in range(GB):
                        c = (g * GB + k) * P
                        last = nc.tensor.transpose(far_t[g % 2][:, k * P:(k + 1) * P], logits[:, c:c + P],
                                                   ident[:, :])
                    last.then_inc(turned, 1)
                    if g > 0:
                        mix_group(g - 1)
                mix_group(GROUPS - 1)


_INS = ['x', 'adj', 'L0_gnn_attn']
_OUTS = [((8192, 128), 'float32')]


def kernel(**inputs):
    import numpy as _np
    import concourse.bacc as _bacc
    from concourse import mybir as _mybir
    from concourse.bass_utils import run_bass_kernel_spmd as _run

    nc = _bacc.Bacc("TRN2", target_bir_lowering=False, num_devices=1)
    arrays, args = {}, []
    for name in _INS:
        a = _np.ascontiguousarray(inputs[name])
        arrays[f"in_{name}_dram"] = a
        args.append(nc.dram_tensor(f"in_{name}_dram", a.shape, _mybir.dt.from_np(a.dtype), kind="ExternalInput").ap())
    for i, (shape, dtype) in enumerate(_OUTS):
        dt = _mybir.dt.from_np(_np.dtype(dtype))
        args.append(nc.dram_tensor(f"out_{i}_dram", shape, dt, kind="ExternalOutput").ap())
    graph_attention_kernel(nc, *args)
    r = _run(nc, [arrays], core_ids=[0])
    return r.results[0]["out_0_dram"]
```

```python
import concourse.bass as bass
from concourse import mybir
from contextlib import ExitStack


def graph_attention_kernel(nc: bass.Bass, x: bass.AP, adj: bass.AP, attn: bass.AP, out: bass.AP):
    fp32, bf16, i32 = mybir.dt.float32, mybir.dt.bfloat16, mybir.dt.int32
    ALU = mybir.AluOpType
    ACT = mybir.ActivationFunctionType
    AX = mybir.AxisListType
    ds = bass.ds

    P = 128
    N, D = x.shape
    TILES = N // P
    PAIRS = TILES // 2
    HALF = N // 2
    CHUNKS = 8
    WORDS = N // CHUNKS
    BANK = 512
    BANKS = WORDS // BANK
    QUARTERS = 4
    PART = WORDS // QUARTERS
    CAND = 8 * QUARTERS
    SLOTS = 8
    BIAS = (2 ** CHUNKS - 1) * WORDS // 2
    COLS = D + 4
    SJ, SI, ONE = D, D + 1, D + 2
    FAR = 2 * N
    MASKED = -1.0e9
    NOTHING = -1.0e30
    EPS = 1e-5
    XC = 4
    XT = TILES // XC
    LC = 8
    RC = 4
    MC = 4
    LW = N // LC
    MW = N // MC
    GB = BANK // P
    GROUPS = N // BANK

    table = nc.dram_tensor("h_table", [N, COLS], fp32).ap()
    sj_row = nc.dram_tensor("sj_row", [TILES, P], fp32).ap()
    row_list = nc.dram_tensor("row_list", [N + P, 1], i32).ap()

    x_t = x.rearrange("(t p) d -> p t d", p=P)
    out_t = out.rearrange("(t p) d -> p t d", p=P)
    adj_t = adj.rearrange("(t p) c -> t p c", p=P)
    table_t = table.rearrange("(t p) c -> p t c", p=P)

    ctx = ExitStack()
    with ctx:
        def sb(name, shape, dt):
            return ctx.enter_context(nc.sbuf_tensor(name, shape, dt))

        def pb(name, shape, dt):
            return ctx.enter_context(nc.psum_tensor(name, shape, dt))

        def sem(name):
            return ctx.enter_context(nc.semaphore(name))

        adj_ring = sb("adj_ring", [P, 4, HALF], i32)
        sign_ring = sb("sign_ring", [P, 4, HALF], bf16)
        h_all = sb("h_all", [P, TILES, COLS], fp32)
        x_all = sb("x_all", [P, TILES, D], fp32)
        near = sb("near", [P, 2, 2 * SLOTS, COLS], fp32)
        mixed_rows = sb("mixed_rows", [P, 2, 2, D], fp32)

        attn_b = sb("attn_b", [P, 2 * D], fp32)
        stats = sb("stats", [P, TILES, 6], fp32)
        mean = sb("mean", [P, TILES], fp32)
        var = sb("var", [P, TILES], fp32)
        gap = sb("gap", [P, TILES], fp32)
        rstd = sb("rstd", [P, TILES], fp32)
        shift = sb("shift", [P, TILES], fp32)
        sj_t = sb("sj_t", [TILES, P], fp32)

        pack_w = sb("pack_w", [P, CHUNKS, P], bf16)
        place_w = sb("place_w", [64, P], bf16)
        place = sb("place", [64, WORDS], bf16)
        before = sb("before", [P, P], bf16)
        ones = sb("ones", [P, P], bf16)
        ident = sb("ident", [P, P], fp32)
        bit_mask = sb("bit_mask", [P, CHUNKS], i32)
        bit_col = sb("bit_col", [P, CHUNKS], i32)
        row_id = sb("row_id", [P, TILES], i32)
        far_row = sb("far_row", [P, TILES + 1], i32)

        cand = sb("cand", [P, 2 * CAND], fp32)
        cand_i = sb("cand_i", [P, 2 * CAND], i32)
        word_at = sb("word_at", [P, 2 * CAND], i32)
        bits = sb("bits", [P, 2, 2 * CAND * CHUNKS], i32)
        cols1 = sb("cols1", [P, 2 * CAND * CHUNKS], fp32)
        hits = sb("hits", [P, 2 * CAND * CHUNKS], fp32)
        best = sb("best", [P, 2 * SLOTS], fp32)
        empty_far = sb("empty_far", [P, 2 * SLOTS], fp32)
        empty_pen = sb("empty_pen", [P, 2, 2 * SLOTS], fp32)
        near_id = sb("near_id", [P, 2, 2 * SLOTS], i32)
        fullest = sb("fullest", [P, 2, 2], fp32)
        count_junk = sb("count_junk", [P, 2, 2 * CAND * CHUNKS], bf16)
        degree = sb("degree", [P, 2, 2], fp32)

        score = sb("score", [P, 2 * SLOTS], fp32)
        leaky = sb("leaky", [P, 2 * SLOTS], fp32)
        top = sb("top", [P, 2], fp32)
        below = sb("below", [P, 2 * SLOTS], fp32)
        weight = sb("weight", [P, 2 * SLOTS], fp32)
        weight_n = sb("weight_n", [P, 2 * SLOTS], fp32)
        total = sb("total", [P, 2], fp32)
        inv = sb("inv", [P, 2], fp32)
        outside = sb("outside", [P, 2], fp32)
        crowded = sb("crowded", [P, 2], fp32)
        flag = sb("flag", [P, 2, 2], bf16)
        flags_before = sb("flags_before", [P, 2, 2], bf16)
        flags_all = sb("flags_all", [P, 1], bf16)
        unlisted = sb("unlisted", [P, 2], fp32)
        list_at = sb("list_at", [P, 2, 2], i32)
        list_row = sb("list_row", [P, 2, 2], i32)
        listed_i = sb("listed_i", [P, 1], i32)
        listed_r = sb("listed_r", [P, 1], i32)
        batches = sb("batches", [P, 1], i32)
        last_batch = sb("last_batch", [P, 1], i32)

        far_id = sb("far_id", [P, 1], i32)
        out_id = sb("out_id", [P, 1], i32)
        far_tab = sb("far_tab", [P, COLS], fp32)
        far_x = sb("far_x", [P, D], fp32)
        part_top = sb("part_top", [P, LC], fp32)
        neg_top = sb("neg_top", [P, 1], fp32)
        p_t = sb("p_t", [P, 2, BANK], fp32)
        far_inv = sb("far_inv", [P, 1], fp32)
        far_out = sb("far_out", [P, D], fp32)

        far_adj = adj_ring[:, 0:2, :].rearrange("p a b -> p (a b)")
        logits = adj_ring[:, 2:4, :].rearrange("p a b -> p (a b)").bitcast(fp32)
        sj_all = sign_ring[:, :, :].rearrange("p a b -> p (a b)").bitcast(fp32)
        mask = x_all[:, :, :].rearrange("p t d -> p (t d)")
        raw = near[:, :, :, :].rearrange("p e k c -> p (e k c)")[:, 0:RC * LW].rearrange("p (r w) -> p r w", r=RC)
        products = near[:, :, :, :].rearrange("p e k c -> p (e k c)")

        words = [pb(f"words{i}", [P, WORDS], fp32) for i in range(2)]
        rank = pb("rank", [P, BANK], fp32)
        far_t = [pb(f"far_t{i}", [P, BANK], fp32) for i in range(2)]
        far_sum = pb("far_sum", [P, BANK], fp32)

        half_neg = sb("half_neg", [P, 1], fp32)

        x_in = [sem(f"x_in{i}") for i in range(XC)]
        attn_in = sem("attn_in")
        adj_in = [sem(f"adj_in{i}") for i in range(4)]
        dve_passed = sem("dve_passed")
        pool_passed = sem("pool_passed")
        setup = sem("setup")
        stat_done = sem("stat_done")
        products_ready = sem("products_ready")
        flag_done = sem("flag_done")
        place_done = sem("place_done")
        std_ready = sem("std_ready")
        h_ready = sem("h_ready")
        table_ready = sem("table_ready")
        sj_turned = sem("sj_turned")
        sj_t_ready = sem("sj_t_ready")
        table_out = sem("table_out")
        sj_out = sem("sj_out")
        consts = sem("consts")
        zeroed = sem("zeroed")
        list_out = sem("list_out")
        signed = sem("signed")
        packed = sem("packed")
        maxed = sem("maxed")
        find = sem("find")
        bits_ready = sem("bits_ready")
        counted = sem("counted")
        near_id_ready = sem("near_id_ready")
        near_in = [sem(f"near_in{i}") for i in range(2)]
        mix = sem("mix")
        below_ready = sem("below_ready")
        weight_ready = sem("weight_ready")
        flags_ready = sem("flags_ready")
        ranked = sem("ranked")
        list_at_ready = sem("list_at_ready")
        list_in = [sem(f"list_in{i}") for i in range(2)]
        pair_mixed = sem("pair_mixed")
        stored = [sem(f"stored{i}") for i in range(2)]
        total_ready = sem("total_ready")
        batches_ready = sem("batches_ready")
        sj_all_in = sem("sj_all_in")
        far_id_in = sem("far_id_in")
        far_tab_in = sem("far_tab_in")
        far_x_in = sem("far_x_in")
        far_adj_in = sem("far_adj_in")
        out_id_in = sem("out_id_in")
        raw_ready = sem("raw_ready")
        masked = sem("masked")
        leaky_done = sem("leaky_done")
        topped = sem("topped")
        long_step = sem("long_step")
        neg_top_ready = sem("neg_top_ready")
        exp_ready = sem("exp_ready")
        turned = sem("turned")
        p_t_ready = sem("p_t_ready")
        p_t_used = sem("p_t_used")
        far_out_ready = sem("far_out_ready")
        far_stored = sem("far_stored")

        FIND = 8
        MIX = 22

        block = ctx.enter_context(nc.Block())

        @block.sync
        def _(sp):
            for c in range(XC):
                sp.dma_start(x_all[:, c * XT:(c + 1) * XT, :], x_t[:, c * XT:(c + 1) * XT, :]).then_inc(x_in[c], 16)
            sp.dma_start(attn_b[:, :], attn.rearrange("d o -> o d").broadcast_to([P, 2 * D])).then_inc(attn_in, 16)

            def load_half(p, s):
                sp.dma_start(adj_ring[:, s, :], adj_t[2 * p + s // 2, :, (s % 2) * HALF:(s % 2 + 1) * HALF]) \
                    .then_inc(adj_in[s], 16)

            def load_pair(p):
                for s in range(4):
                    sp.wait_ge(signed, 4 * p + s - 3)
                    load_half(p, s)

            def store_pair(q, e):
                sp.wait_ge(pair_mixed, q + 1)
                sp.dma_start(out_t[:, ds(2 * q, 2), :], mixed_rows[:, e, :, :]).then_inc(stored[e], 16)

            for s in range(4):
                load_half(0, s)
            load_pair(1)
            load_pair(2)
            load_pair(3)
            store_pair(0, 0)
            with sp.Fori(2, PAIRS // 2) as i:
                for e in range(2):
                    load_pair(2 * i + e)
                    store_pair(2 * i + e - 3, (e + 1) % 2)
            for q in range(PAIRS - 3, PAIRS):
                store_pair(q, q % 2)
                if q == PAIRS - 3:
                    sp.wait_ge(packed, 4 * PAIRS)
                    sp.wait_ge(sj_out, 16)
                    sp.dma_start(sj_all, sj_row.rearrange("t p -> (t p)").rearrange("(o n) -> o n", o=1)
                                 .broadcast_to([P, N])).then_inc(sj_all_in, 16)

        @block.gpsimd
        def _(pool):
            nc.gpsimd.memset(ident[:, :], 0.0)
            nc.gpsimd.memset(ones[:, :], 1.0)
            nc.gpsimd.memset(pack_w[:, :, :], 0.0)
            nc.gpsimd.memset(place_w[:, :], 1.0)
            nc.gpsimd.memset(place[:, :], 0.0)
            nc.gpsimd.memset(far_row[:, :], FAR).then_inc(zeroed, 1)
            pool.wait_ge(zeroed, 1)
            nc.gpsimd.affine_select(out=ident[:, :], in_=ident[:, :], compare_op=ALU.not_equal, fill=1.0,
                                    base=0, pattern=[[-1, P]], channel_multiplier=1)
            nc.gpsimd.affine_select(out=before[:, :], in_=ones[:, :], compare_op=ALU.is_gt, fill=0.0,
                                    base=0, pattern=[[1, P]], channel_multiplier=-1)
            for c in range(CHUNKS):
                last = nc.gpsimd.affine_select(out=pack_w[:, c, :], in_=pack_w[:, c, :], compare_op=ALU.not_equal,
                                               fill=float(2 ** c * WORDS // 2), base=0, pattern=[[-1, P]],
                                               channel_multiplier=1)
            last.then_inc(zeroed, 1)
            pool.wait_ge(zeroed, 2)
            nc.gpsimd.iota(place[0:32, :], pattern=[[1, WORDS // 32], [0, 32]], base=0, channel_multiplier=0,
                           allow_small_or_imprecise_dtypes=True).then_inc(zeroed, 1)
            pool.wait_ge(zeroed, 3)
            nc.gpsimd.iota(place[32:33, :], pattern=[[0, WORDS // 32], [1, 32]], base=0, channel_multiplier=0,
                           allow_small_or_imprecise_dtypes=True).then_inc(zeroed, 1)
            pool.wait_ge(zeroed, 4)
            for c in range(CHUNKS):
                nc.gpsimd.memset(bit_mask[:, c:c + 1], 2 ** c * WORDS)
            nc.gpsimd.iota(bit_col[:, :], pattern=[[WORDS, CHUNKS]], base=1, channel_multiplier=0)
            nc.gpsimd.memset(near[:, :, :, :], 0.0)
            nc.gpsimd.memset(far_tab[:, :], 0.0)
            nc.gpsimd.memset(far_x[:, :], 0.0)
            nc.gpsimd.memset(half_neg[:, :], -0.5)
            nc.gpsimd.iota(row_id[:, :], pattern=[[P, TILES]], base=0, channel_multiplier=1).then_inc(consts, 1)
            pool.wait_ge(consts, 1)
            pool.dma_start(row_list.rearrange("(p t) o -> p (t o)", p=P), far_row[:, :]).then_inc(list_out, 16)
            for c in range(XC):
                pool.wait_ge(table_ready, c + 1)
                pool.dma_start(table_t[:, c * XT:(c + 1) * XT, :], h_all[:, c * XT:(c + 1) * XT, :]) \
                    .then_inc(table_out, 16)
            pool.wait_ge(sj_t_ready, 1)
            pool.dma_start(sj_row, sj_t[:, :]).then_inc(sj_out, 16)
            pool.wait_ge(list_out, 16)
            pool.wait_ge(table_out, 16 * XC)

            last_row = pool.to_reg(N - 1)

            def gather_pair(p, e):
                pool.wait_ge(near_id_ready, p + 1)
                pool.sem_inc(pool_passed, 1)
                for k in range(2 * SLOTS):
                    pool.indirect_dma_start(
                        out=near[:, e, k, :], out_offset=None, in_=table,
                        in_offset=bass.IndirectOffsetOnAxis(ap=near_id[:, e, k:k + 1], axis=0),
                        bounds_check=last_row, oob_is_err=False).then_inc(near_in[e], 16)

            def list_pair(q, e):
                pool.wait_ge(list_at_ready, q + 1)
                pool.sem_inc(pool_passed, 1)
                for a in range(2):
                    pool.indirect_dma_start(
                        out=row_list, out_offset=bass.IndirectOffsetOnAxis(ap=list_at[:, e, a:a + 1], axis=0),
                        in_=list_row[:, e, a:a + 1], in_offset=None,
                        bounds_check=last_row, oob_is_err=False).then_inc(list_in[e], 16)

            gather_pair(0, 0)
            gather_pair(1, 1)
            with pool.Fori(1, PAIRS // 2) as i:
                for e in range(2):
                    pool.wait_ge(pair_mixed, 2 * i + e - 1)
                    gather_pair(2 * i + e, e)
                    list_pair(2 * i + e - 2, e)
            list_pair(PAIRS - 2, 0)
            list_pair(PAIRS - 1, 1)

            for e in range(2):
                pool.wait_ge(list_in[e], 16 * PAIRS)
                pool.wait_ge(stored[e], 8 * PAIRS)
            pool.wait_ge(signed, 4 * PAIRS)
            pool.wait_ge(batches_ready, 1)
            n_batches = pool.value_load(batches[0:1, 0:1], min_val=2, max_val=TILES)

            def far_gather(dst, src, ids, done):
                pool.indirect_dma_start(
                    out=dst, out_offset=None, in_=src, in_offset=bass.IndirectOffsetOnAxis(ap=ids[:, 0:1], axis=0),
                    bounds_check=last_row, oob_is_err=False).then_inc(done, 16)

            def fetch(b):
                pool.dma_start(far_id[:, :], row_list[ds(b * P, P), :]).then_inc(far_id_in, 16)
                pool.wait_ge(far_id_in, 16 * b + 16)
                pool.sem_inc(pool_passed, 1)
                far_gather(far_tab[:, :], table, far_id, far_tab_in)
                far_gather(far_adj, adj, far_id, far_adj_in)

            def fetch_x(b):
                pool.dma_start(out_id[:, :], row_list[ds(b * P, P), :]).then_inc(out_id_in, 16)
                pool.wait_ge(out_id_in, 16 * b + 16)
                pool.sem_inc(pool_passed, 1)
                far_gather(far_x[:, :], x, out_id, far_x_in)

            def store_far(b):
                pool.wait_ge(far_out_ready, b + 1)
                pool.sem_inc(pool_passed, 1)
                pool.indirect_dma_start(
                    out=out, out_offset=bass.IndirectOffsetOnAxis(ap=out_id[:, 0:1], axis=0),
                    in_=far_out[:, :], in_offset=None,
                    bounds_check=last_row, oob_is_err=False).then_inc(far_stored, 16)

            fetch(0)
            fetch_x(0)
            with pool.Fori(1, n_batches) as b:
                pool.wait_ge(masked, MC * b)
                pool.wait_ge(raw_ready, LC * b)
                pool.sem_inc(pool_passed, 1)
                fetch(b)
                store_far(b - 1)
                pool.wait_ge(far_stored, 16 * b)
                pool.sem_inc(pool_passed, 1)
                fetch_x(b)
            store_far(n_batches - 1)
            pool.wait_ge(far_stored, 16 * n_batches)

        @block.scalar
        def _(act):
            act.wait_ge(consts, 1)

            def sign_tile(p, a, first=False):
                for s in (2 * a, 2 * a + 1):
                    act.wait_ge(adj_in[s], 16 * p + 16)
                    if not first:
                        act.wait_ge(packed, 4 * p + s - 3)
                    nc.scalar.activation(sign_ring[:, s, :], adj_ring[:, s, :], ACT.Sign, bias=half_neg[:, :]) \
                        .then_inc(signed, 1)

            def count_pair(p, e):
                act.wait_ge(bits_ready, p + 1)
                w = CAND * CHUNKS
                for a in range(2):
                    nc.scalar.activation(count_junk[:, e, a * w:(a + 1) * w], bits[:, e, a * w:(a + 1) * w], ACT.Sign,
                                         accum_out=degree[:, e, a:a + 1]).then_inc(counted, 1)

            def exp_pair(p):
                act.wait_ge(below_ready, p + 1)
                nc.scalar.activation(weight[:, :], below[:, :], ACT.Exp).then_inc(weight_ready, 1)

            act.wait_ge(setup, 8)
            nc.scalar.activation(rstd[:, :], var[:, :], ACT.Sqrt).then_inc(std_ready, 1)
            act.wait_ge(setup, 10)
            for c in range(XC):
                with act.Fori(c * XT // 4, (c + 1) * XT // 4) as i:
                    for u in range(4):
                        t = 4 * i + u
                        nc.scalar.activation(h_all[:, t, 0:D], x_all[:, t, :], ACT.Relu,
                                             bias=shift[:, ds(t, 1)], scale=rstd[:, ds(t, 1)]) \
                            .then_inc(h_ready, 1)
                sign_tile(c // 2, c % 2, c < 2)
            count_pair(0, 0)
            with act.Fori(1, PAIRS // 2) as i:
                for e in range(2):
                    sign_tile(2 * i + e, 0)
                    exp_pair(2 * i + e - 2)
                    sign_tile(2 * i + e, 1)
                    count_pair(2 * i + e - 1, (e + 1) % 2)
            exp_pair(PAIRS - 2)
            count_pair(PAIRS - 1, 1)
            exp_pair(PAIRS - 1)

            act.wait_ge(sj_all_in, 16)
            act.wait_ge(packed, 4 * PAIRS)
            act.wait_ge(batches_ready, 1)
            n_batches = act.value_load(batches[0:1, 0:1], min_val=2, max_val=TILES)

            def raw_chunk(b, c):
                if c >= RC:
                    act.wait_ge(topped, LC * b + c - RC + 1)
                nc.scalar.activation(raw[:, c % RC, :], sj_all[:, c * LW:(c + 1) * LW], ACT.Identity,
                                     bias=far_tab[:, SI:SI + 1]).then_inc(raw_ready, 1)

            def exp_chunks(b):
                act.wait_ge(neg_top_ready, b + 1)
                for c in range(LC):
                    nc.scalar.activation(logits[:, c * LW:(c + 1) * LW], logits[:, c * LW:(c + 1) * LW], ACT.Exp,
                                         bias=neg_top[:, 0:1]).then_inc(exp_ready, 1)

            def evacuate(b, g):
                act.wait_ge(turned, GROUPS * b + g + 1)
                if g >= 2:
                    act.wait_ge(p_t_used, GROUPS * b + g - 1)
                nc.scalar.activation(p_t[:, g % 2, :], far_t[g % 2][:, :], ACT.Copy).then_inc(p_t_ready, 1)

            act.wait_ge(far_tab_in, 16)
            for c in range(LC):
                raw_chunk(0, c)
            exp_chunks(0)
            with act.Fori(1, n_batches) as b:
                for c in range(LC):
                    for g in range(c * GROUPS // LC, (c + 1) * GROUPS // LC):
                        evacuate(b - 1, g)
                    if c == 0:
                        act.wait_ge(far_tab_in, 16 * b + 16)
                    raw_chunk(b, c)
                exp_chunks(b)
            last_b = act.value_load(last_batch[0:1, 0:1], min_val=1, max_val=TILES - 1)
            for g in range(GROUPS):
                evacuate(last_b, g)

        @block.vector
        def _(dve):
            for c in range(XC):
                dve.wait_ge(x_in[c], 16)
                with dve.Fori(c * XT // 4, (c + 1) * XT // 4) as i:
                    for u in range(4):
                        nc.vector.bn_stats(out=stats[:, 4 * i + u, :], in_=x_all[:, 4 * i + u, :]) \
                            .then_inc(stat_done, 1)
            dve.wait_ge(stat_done, TILES)
            nc.vector.tensor_tensor(mean[:, :], stats[:, :, 1], stats[:, :, 4], ALU.add).then_inc(setup, 1)
            nc.vector.tensor_tensor(gap[:, :], stats[:, :, 1], stats[:, :, 4], ALU.subtract).then_inc(setup, 1)
            nc.vector.tensor_tensor(var[:, :], stats[:, :, 2], stats[:, :, 5], ALU.add).then_inc(setup, 1)
            dve.wait_ge(setup, 3)
            nc.vector.tensor_tensor(gap[:, :], gap[:, :], gap[:, :], ALU.mult).then_inc(setup, 1)
            nc.vector.tensor_scalar(mean[:, :], mean[:, :], 0.5, None, ALU.mult).then_inc(setup, 1)
            nc.vector.tensor_scalar(var[:, :], var[:, :], 1.0 / D, EPS, ALU.mult, ALU.add).then_inc(setup, 1)
            dve.wait_ge(setup, 6)
            nc.vector.tensor_scalar(gap[:, :], gap[:, :], 0.25, None, ALU.mult).then_inc(setup, 1)
            dve.wait_ge(setup, 7)
            nc.vector.tensor_tensor(var[:, :], var[:, :], gap[:, :], ALU.add).then_inc(setup, 1)
            dve.wait_ge(std_ready, 1)
            nc.vector.reciprocal(rstd[:, :], rstd[:, :]).then_inc(setup, 1)
            dve.wait_ge(setup, 9)
            nc.vector.scalar_tensor_tensor(shift[:, :], mean[:, :], -1.0, rstd[:, :], ALU.mult, ALU.mult) \
                .then_inc(setup, 1)
            dve.wait_ge(attn_in, 16)
            dve.wait_ge(consts, 1)
            nc.vector.memset(h_all[:, :, ONE:ONE + 1], 1.0)
            nc.vector.memset(h_all[:, :, ONE + 1:ONE + 2], 0.0)
            nc.vector.memset(flags_all[:, :], 0.0)
            for c in range(XC):
                dve.wait_ge(h_ready, (c + 1) * XT)
                if c > 0:
                    dve.wait_ge(table_ready, c)
                prods = [products[:, a * XT * D:(a + 1) * XT * D].rearrange("p (t d) -> p t d", d=D)
                         for a in range(2)]
                for a in range(2):
                    nc.vector.tensor_tensor(
                        prods[a], h_all[:, c * XT:(c + 1) * XT, 0:D],
                        attn_b[:, a * D:(a + 1) * D].unsqueeze(1).broadcast_to([P, XT, D]), ALU.mult) \
                        .then_inc(products_ready, 1)
                for a, col in ((0, SI), (1, SJ)):
                    dve.wait_ge(products_ready, 2 * c + a + 1)
                    last = nc.vector.tensor_reduce(h_all[:, c * XT:(c + 1) * XT, col], prods[a], AX.X, ALU.add)
                last.then_inc(table_ready, 1)
            dve.wait_ge(sj_turned, 1)
            nc.vector.tensor_copy(sj_t[:, :], rank[0:TILES, 0:P]).then_inc(sj_t_ready, 1)

            def find_pair(p, e):
                f = FIND * p
                for a in range(2):
                    dve.wait_ge(packed, 4 * p + 2 * a + 2)
                    dve.sem_inc(dve_passed, 1)
                    for q in range(QUARTERS):
                        last = nc.vector.max(out=cand[:, a * CAND + 8 * q:a * CAND + 8 * q + 8],
                                             in_=words[a][:, q * PART:(q + 1) * PART])
                    last.then_inc(maxed, 1)
                dve.wait_ge(maxed, 2 * p + 2)
                nc.vector.tensor_scalar(cand_i[:, :], cand[:, :], float(BIAS), None, ALU.add).then_inc(find, 1)
                least = cand[:, :].rearrange("p (a q k) -> p a q k", a=2, k=8)[:, :, :, 7]
                nc.vector.tensor_reduce(fullest[:, e, :], least, AX.X, ALU.max).then_inc(find, 1)
                dve.wait_ge(find, f + 2)
                word = cand_i[:, :].unsqueeze(2).broadcast_to([P, 2 * CAND, CHUNKS])
                nc.vector.tensor_tensor(
                    bits[:, e, :].rearrange("p (w c) -> p w c", c=CHUNKS), word,
                    bit_mask[:, :].unsqueeze(1).broadcast_to([P, 2 * CAND, CHUNKS]), ALU.bitwise_and) \
                    .then_inc(bits_ready, 1)
                nc.vector.tensor_scalar(word_at[:, :], cand_i[:, :], WORDS - 1, None, ALU.bitwise_and) \
                    .then_inc(find, 1)
                dve.wait_ge(find, f + 3)
                nc.vector.tensor_tensor(
                    cols1[:, :].rearrange("p (w c) -> p w c", c=CHUNKS),
                    word_at[:, :].unsqueeze(2).broadcast_to([P, 2 * CAND, CHUNKS]),
                    bit_col[:, :].unsqueeze(1).broadcast_to([P, 2 * CAND, CHUNKS]), ALU.add).then_inc(find, 1)
                dve.wait_ge(find, f + 4)
                dve.wait_ge(bits_ready, p + 1)
                nc.vector.scalar_tensor_tensor(hits[:, :], bits[:, e, :], 0.0, cols1[:, :], ALU.is_gt, ALU.mult) \
                    .then_inc(find, 1)
                dve.wait_ge(find, f + 5)
                dve.sem_inc(dve_passed, 1)
                w = CAND * CHUNKS
                for a in range(2):
                    last = nc.vector.max(out=best[:, a * SLOTS:(a + 1) * SLOTS], in_=hits[:, a * w:(a + 1) * w])
                last.then_inc(find, 1)
                dve.wait_ge(find, f + 6)
                nc.vector.tensor_scalar(empty_pen[:, e, :], best[:, :], 0.0, NOTHING, ALU.is_equal, ALU.mult) \
                    .then_inc(find, 1)
                nc.vector.tensor_scalar(empty_far[:, :], best[:, :], 0.0, float(FAR), ALU.is_equal, ALU.mult) \
                    .then_inc(find, 1)
                dve.wait_ge(find, f + 8)
                nc.vector.scalar_tensor_tensor(near_id[:, e, :], best[:, :], -1.0, empty_far[:, :],
                                               ALU.add, ALU.add).then_inc(near_id_ready, 1)

            def list_places(q, e, reuse=True):
                dve.wait_ge(ranked, q + 1)
                if reuse:
                    dve.wait_ge(list_in[e], 16 * q - 16 * e)
                nc.vector.tensor_scalar(unlisted[:, :], flag[:, e, :], float(-FAR), float(FAR), ALU.mult, ALU.add) \
                    .then_inc(place_done, 1)
                nc.vector.tensor_copy(list_row[:, e, :], row_id[:, ds(2 * q, 2)]).then_inc(place_done, 1)
                dve.wait_ge(place_done, 2 * q + 2)
                nc.vector.tensor_tensor(list_at[:, e, :], unlisted[:, :], rank[:, 2 * e:2 * e + 2], ALU.add) \
                    .then_inc(list_at_ready, 1)

            def mix_pair(q, e, first=False, reuse=True, reuse_places=True):
                m = MIX * q
                dve.wait_ge(near_in[e], 128 * q + (256 if e == 0 else 128))
                s_near = near[:, e, :, SJ].rearrange("p (a k) -> p a k", a=2)
                s_own = h_all[:, ds(2 * q, 2), SI:SI + 1].broadcast_to([P, 2, SLOTS])
                nc.vector.tensor_tensor(score[:, :].rearrange("p (a k) -> p a k", a=2), s_near, s_own, ALU.add) \
                    .then_inc(mix, 1)
                dve.wait_ge(mix, m + 1)
                nc.vector.tensor_tensor(score[:, :], score[:, :], empty_pen[:, e, :], ALU.add).then_inc(mix, 1)
                dve.wait_ge(mix, m + 2)
                nc.vector.scalar_tensor_tensor(leaky[:, :], score[:, :], 0.2, score[:, :], ALU.mult, ALU.max) \
                    .then_inc(mix, 1)
                dve.wait_ge(mix, m + 3)
                leaky_k = leaky[:, :].rearrange("p (a k) -> p a k", a=2)
                nc.vector.tensor_reduce(top[:, :], leaky_k, AX.X, ALU.max).then_inc(mix, 1)
                dve.wait_ge(mix, m + 4)
                nc.vector.tensor_tensor(below[:, :].rearrange("p (a k) -> p a k", a=2), leaky_k,
                                        top[:, :].unsqueeze(2).broadcast_to([P, 2, SLOTS]), ALU.subtract) \
                    .then_inc(below_ready, 1)

                dve.wait_ge(counted, 2 * q + 2)
                nc.vector.scalar_tensor_tensor(outside[:, :], degree[:, e, :], -float(SLOTS + 1), degree[:, e, :],
                                               ALU.add, ALU.mult).then_inc(flag_done, 1)
                nc.vector.tensor_scalar(crowded[:, :], fullest[:, e, :], float(WORDS - BIAS), None, ALU.is_ge) \
                    .then_inc(flag_done, 1)
                dve.wait_ge(flag_done, 5 * q + 2)
                nc.vector.scalar_tensor_tensor(flag[:, e, :], outside[:, :], 0.0, crowded[:, :],
                                               ALU.is_ge, ALU.max).then_inc(flag_done, 1)
                nc.vector.tensor_copy(flags_before[:, e, 0:1], flags_all[:, :]).then_inc(flag_done, 1)
                dve.wait_ge(flag_done, 5 * q + 4)
                nc.vector.tensor_tensor(flags_before[:, e, 1:2], flags_all[:, :], flag[:, e, 0:1], ALU.add) \
                    .then_inc(flag_done, 1)
                dve.wait_ge(flag_done, 5 * q + 5)
                nc.vector.tensor_tensor(flags_all[:, :], flags_before[:, e, 1:2], flag[:, e, 1:2], ALU.add) \
                    .then_inc(flags_ready, 1)
                if not first:
                    list_places(q - 1, 1 - e, reuse_places)

                dve.wait_ge(weight_ready, q + 1)
                weight_k = weight[:, :].rearrange("p (a k) -> p a k", a=2)
                nc.vector.tensor_reduce(total[:, :], weight_k, AX.X, ALU.add).then_inc(mix, 1)
                dve.wait_ge(mix, m + 5)
                nc.vector.reciprocal(inv[:, :], total[:, :]).then_inc(mix, 1)
                dve.wait_ge(mix, m + 6)
                nc.vector.tensor_tensor(weight_n[:, :].rearrange("p (a k) -> p a k", a=2), weight_k,
                                        inv[:, :].unsqueeze(2).broadcast_to([P, 2, SLOTS]), ALU.mult) \
                    .then_inc(mix, 1)
                dve.wait_ge(mix, m + 7)
                if reuse:
                    dve.wait_ge(stored[e], 8 * q - 8 * e)
                done = 7
                for k in range(SLOTS):
                    for a in range(2):
                        acc = mixed_rows[:, e, a, :]
                        base = x_all[:, 2 * q + a, :] if k == 0 else acc
                        if k > 0:
                            dve.wait_ge(mix, m + done - 1)
                        ins = nc.vector.scalar_tensor_tensor(
                            acc, near[:, e, a * SLOTS + k, 0:D], weight_n[:, a * SLOTS + k:a * SLOTS + k + 1], base,
                            ALU.mult, ALU.add)
                        final = k == SLOTS - 1 and a == 1
                        ins.then_inc(pair_mixed if final else mix, 1)
                        done += 1
                assert done - 1 == MIX

            find_pair(0, 0)
            find_pair(1, 1)
            mix_pair(0, 0, first=True, reuse=False)
            find_pair(2, 0)
            mix_pair(1, 1, reuse=False, reuse_places=False)
            find_pair(3, 1)
            mix_pair(2, 0, reuse_places=False)
            with dve.Fori(2, PAIRS // 2) as i:
                find_pair(2 * i, 0)
                mix_pair(2 * i - 1, 1)
                find_pair(2 * i + 1, 1)
                mix_pair(2 * i, 0)
            mix_pair(PAIRS - 1, 1)
            list_places(PAIRS - 1, 1)

            dve.wait_ge(total_ready, 1)
            nc.vector.tensor_scalar(listed_i[:, :], rank[:, 8:9], float(P - 1), float(2 * P), ALU.add, ALU.max) \
                .then_inc(long_step, 1)
            dve.wait_ge(long_step, 1)
            nc.vector.tensor_scalar(batches[:, :], listed_i[:, :], P.bit_length() - 1, None,
                                    ALU.arith_shift_right).then_inc(long_step, 1)
            dve.wait_ge(long_step, 2)
            nc.vector.tensor_scalar(last_batch[:, :], batches[:, :], -1.0, None, ALU.add).then_inc(batches_ready, 1)

            dve.wait_ge(batches_ready, 1)
            n_batches = dve.value_load(batches[0:1, 0:1], min_val=2, max_val=TILES)

            def top_chunk(b, c, first):
                dve.wait_ge(leaky_done, LC * b + c + 1)
                if not first:
                    dve.wait_ge(turned, GROUPS * (b - 1) + (c + 1) * GROUPS // LC)
                dve.sem_inc(dve_passed, 1)
                nc.vector.tensor_tensor_reduce(
                    out=logits[:, c * LW:(c + 1) * LW], in0=raw[:, c % RC, :], in1=mask[:, c * LW:(c + 1) * LW],
                    scale=1.0, scalar=-3.0e38, op0=ALU.add, op1=ALU.max,
                    accum_out=part_top[:, c:c + 1]).then_inc(topped, 1)

            def front(b, first=False):
                dve.wait_ge(far_adj_in, 16 * b + 16)
                for m in range(MC):
                    nc.vector.tensor_scalar(mask[:, m * MW:(m + 1) * MW], far_adj[:, m * MW:(m + 1) * MW], 0.0,
                                            MASKED, ALU.is_le, ALU.mult).then_inc(masked, 1)
                dve.wait_ge(masked, MC * b + MC)
                for c in range(LC):
                    dve.wait_ge(raw_ready, LC * b + c + 1)
                    nc.vector.scalar_tensor_tensor(raw[:, c % RC, :], raw[:, c % RC, :], 0.2, raw[:, c % RC, :],
                                                   ALU.mult, ALU.max).then_inc(leaky_done, 1)
                    if c > 0:
                        top_chunk(b, c - 1, first)
                top_chunk(b, LC - 1, first)
                dve.wait_ge(topped, LC * b + LC)
                nc.vector.tensor_reduce(neg_top[:, :], part_top[:, :], AX.X, ALU.max, negate=True) \
                    .then_inc(neg_top_ready, 1)

            def finish(b):
                dve.wait_ge(p_t_used, GROUPS * b + GROUPS)
                nc.vector.reciprocal(far_inv[:, :], far_sum[:, ONE:ONE + 1]).then_inc(long_step, 1)
                dve.wait_ge(long_step, b + 3)
                dve.wait_ge(far_x_in, 16 * b + 16)
                nc.vector.scalar_tensor_tensor(far_out[:, :], far_sum[:, 0:D], far_inv[:, 0:1], far_x[:, :],
                                               ALU.mult, ALU.add).then_inc(far_out_ready, 1)

            front(0, True)
            with dve.Fori(1, n_batches) as b:
                front(b)
                finish(b - 1)
            finish(n_batches - 1)

        @block.tensor
        def _(pe):
            pe.wait_ge(consts, 1)
            def pack_tile(p, a, first=False):
                if not first:
                    pe.wait_ge(maxed, 2 * p + a - 1)
                for k in range(BANKS):
                    nc.tensor.matmul(words[a][:, k * BANK:(k + 1) * BANK], place_w[:, :],
                                     place[:, k * BANK:(k + 1) * BANK], start=True, stop=False)
                for c in range(CHUNKS):
                    s, o = 2 * a + c // (CHUNKS // 2), (c % (CHUNKS // 2)) * WORDS
                    if c % (CHUNKS // 2) == 0:
                        pe.wait_ge(signed, 4 * p + s + 1)
                    for k in range(BANKS):
                        last = nc.tensor.matmul(words[a][:, k * BANK:(k + 1) * BANK], pack_w[:, c, :],
                                                sign_ring[:, s, o + k * BANK:o + (k + 1) * BANK],
                                                start=False, stop=(c == CHUNKS - 1))
                    if c % (CHUNKS // 2) == CHUNKS // 2 - 1:
                        last.then_inc(packed, 1)

            def rank_pair(q, e, first=False):
                pe.wait_ge(flags_ready, q + 1)
                if first:
                    pe.wait_ge(sj_t_ready, 1)
                else:
                    pe.wait_ge(list_at_ready, q)
                at = rank[:, 2 * e:2 * e + 2]
                nc.tensor.matmul(at, before[:, :], flag[:, e, :], start=True, stop=False)
                nc.tensor.matmul(at, ones[:, :], flags_before[:, e, :], start=False, stop=True).then_inc(ranked, 1)

            pack_tile(0, 0, True)
            pack_tile(0, 1, True)
            pe.wait_ge(table_ready, XC)
            nc.tensor.transpose(rank[0:TILES, 0:P], h_all[:, :, SJ], ident[:, :]).then_inc(sj_turned, 1)
            pack_tile(1, 0)
            pack_tile(1, 1)
            pack_tile(2, 0)
            pack_tile(2, 1)
            rank_pair(0, 0, True)
            with pe.Fori(1, PAIRS // 2 - 1) as i:
                for e in (1, 0):
                    pack_tile(2 * i + 2 - e, 0)
                    pack_tile(2 * i + 2 - e, 1)
                    rank_pair(2 * i - e, e)
            pack_tile(PAIRS - 1, 0)
            pack_tile(PAIRS - 1, 1)
            rank_pair(PAIRS - 3, 1)
            rank_pair(PAIRS - 2, 0)
            rank_pair(PAIRS - 1, 1)
            pe.wait_ge(flags_ready, PAIRS)
            pe.wait_ge(list_at_ready, PAIRS)
            nc.tensor.matmul(rank[:, 8:9], ones[:, :], flags_all[:, :], start=True, stop=True) \
                .then_inc(total_ready, 1)

            pe.wait_ge(batches_ready, 1)
            n_batches = pe.value_load(batches[0:1, 0:1], min_val=2, max_val=TILES)

            def turn_group(b, g):
                pe.wait_ge(exp_ready, LC * b + g * LC // GROUPS + 1)
                for k in range(GB):
                    c = (g * GB + k) * P
                    last = nc.tensor.transpose(far_t[g % 2][:, k * P:(k + 1) * P], logits[:, c:c + P], ident[:, :])
                last.then_inc(turned, 1)

            def mix_group(b, g):
                pe.wait_ge(p_t_ready, GROUPS * b + g + 1)
                for k in range(GB):
                    t = g * GB + k
                    last = nc.tensor.matmul(far_sum[:, 0:ONE + 1], p_t[:, g % 2, k * P:(k + 1) * P],
                                            h_all[:, t, 0:ONE + 1], start=(t == 0), stop=(t == TILES - 1))
                last.then_inc(p_t_used, 1)

            def back(b, first=False):
                for g in range(GROUPS):
                    turn_group(b, g)
                    if g == 1 and not first:
                        pe.wait_ge(far_out_ready, b)
                    if g > 0:
                        mix_group(b, g - 1)
                mix_group(b, GROUPS - 1)

            back(0, True)
            with pe.Fori(1, n_batches) as b:
                back(b)


_INS = ['x', 'adj', 'L0_gnn_attn']
_OUTS = [((8192, 128), 'float32')]


def kernel(**inputs):
    import numpy as _np
    import concourse.bacc as _bacc
    from concourse import mybir as _mybir
    from concourse.bass_utils import run_bass_kernel_spmd as _run

    nc = _bacc.Bacc("TRN2", target_bir_lowering=False, num_devices=1)
    arrays, args = {}, []
    for name in _INS:
        a = _np.ascontiguousarray(inputs[name])
        arrays[f"in_{name}_dram"] = a
        args.append(nc.dram_tensor(f"in_{name}_dram", a.shape, _mybir.dt.from_np(a.dtype), kind="ExternalInput").ap())
    for i, (shape, dtype) in enumerate(_OUTS):
        dt = _mybir.dt.from_np(_np.dtype(dtype))
        args.append(nc.dram_tensor(f"out_{i}_dram", shape, dt, kind="ExternalOutput").ap())
    graph_attention_kernel(nc, *args)
    r = _run(nc, [arrays], core_ids=[0])
    return r.results[0]["out_0_dram"]
```
